# Optimizing a Trainium2 kernel written in Bass

```python
import numpy as np
import jax
import jax.numpy as jnp

def _softmax(x, axis=-1):
    return jax.nn.softmax(x, axis=axis)

def _gelu(x):
    return jax.nn.gelu(x, approximate=True)

def _silu(x):
    return jax.nn.silu(x)

def _sigmoid(x):
    return jax.nn.sigmoid(x)

def _layernorm(x, axis=-1, eps=1e-05):
    m = jnp.mean(x, axis=axis, keepdims=True)
    v = jnp.var(x, axis=axis, keepdims=True)
    return (x - m) / jnp.sqrt(v + eps)

def _scatter_add(tgt, idx, src, axis=0):
    return tgt.at[idx].add(src)

def _segment_sum(src, seg, n):
    return jax.ops.segment_sum(src, seg, n)
kernel_name = 'mk_rec_standalone_d1_rec_r8_e64205'

def setup_inputs(seed: int=0):
    np.random.seed(seed)
    _w = jnp.asarray

    def _rec_inputs():
        import jax
        import jax.numpy as jnp
        _rk = jax.random.key(seed)
        r_inputs = -0.000718957 + 1.00057 * jax.random.normal(jax.random.fold_in(_rk, 1), (2048, 40, 64), jnp.float32)
        return r_inputs
    r_inputs = _rec_inputs()

    def _L0_rec_setup():
        import jax, jax.numpy as jnp
        import numpy as np
        B, N, E = (1024, 40, 64)
        P = N * (N - 1) // 2

        def _pair_indices(n):
            row, col = ([], [])
            for i in range(n - 1):
                for j in range(i + 1, n):
                    row.append(i)
                    col.append(j)
            return (np.asarray(row), np.asarray(col))
        key = jax.random.key(seed)
        k1, k2 = jax.random.split(key)
        inputs = jax.random.normal(k1, (B, N, E), dtype=jnp.float32)
        std = float(np.sqrt(2.0 / (E + E)))
        param = jax.random.normal(k2, (E, P, E), dtype=jnp.float32) * std
        return {'inputs': inputs, 'param': param}
    _L0_rec_all = _L0_rec_setup()
    _L0_rec_in = {k: v for k, v in _L0_rec_all.items() if k in ('param',)}
    del _L0_rec_all
    return {'r_inputs': r_inputs, 'L0_rec_param': _L0_rec_in['param']}

def reference(r_inputs, L0_rec_param):
    import jax
    import jax.numpy as jnp

    def _L0_rec_ref(inputs, param):
        import jax, jax.numpy as jnp
        import numpy as np
        B, N, E = (1024, 40, 64)
        P = N * (N - 1) // 2

        def _pair_indices(n):
            row, col = ([], [])
            for i in range(n - 1):
                for j in range(i + 1, n):
                    row.append(i)
                    col.append(j)
            return (np.asarray(row), np.asarray(col))
        n = inputs.shape[1]
        rowidx, colidx = _pair_indices(n)
        p = inputs[:, rowidx]
        q = inputs[:, colidx]
        out = jnp.einsum('bie,fie,bif->bi', p, param, q)
        return out[:, None, :]
    y = _L0_rec_ref(r_inputs, L0_rec_param)
    return y

_drawn_inputs = setup_inputs


def setup_inputs(seed=0):
    import zlib

    import numpy as np

    out = dict(_drawn_inputs(seed))
    spreads = {}
    factors = {}
    for name, (base, spread) in spreads.items():
        noise = np.random.default_rng([zlib.crc32(name.encode()), seed]).standard_normal(out[name].shape)
        drawn = base * np.exp(spread * noise) if base else spread * noise
        out[name] = jnp.asarray(drawn.astype(out[name].dtype))
    for name, factor in factors.items():
        out[name] = (out[name] * factor).astype(out[name].dtype)
    return out
```

```python
from contextlib import ExitStack

import concourse.bass as bass
from concourse import mybir
from concourse.alu_op_type import AluOpType as ALU

F32 = mybir.dt.float32
F32R = mybir.dt.float32r
ACT = mybir.ActivationFunctionType

P = 128
BLK = 8
NJ = BLK // 2
BANK = 512
HALF = 1024
NC = HALF // BANK

LAST = [(2, 6), (3, 7)]
RECT = [(j, d) for j in range(NJ) for d in range(BLK) if (j, d) not in LAST] + LAST
DIAG = [(0, 1), (0, 2), (0, 3), (0, 4), (0, 5), (0, 6), (0, 7), (1, 4), (1, 3), (1, 6), (1, 5), (1, 7),
        (2, 5), (2, 7)] + LAST


def last_use(units, what, value):
    return max([s for s, u in enumerate(units) if u[what] == value], default=-1)


def build(nc, x, w, out):
    B, N, E = x.shape
    NPAIR = w.shape[1]
    assert E * 2 == P and N % BLK == 0 and B % HALF == 0 and NPAIR == N * (N - 1) // 2
    ROWS = N // BLK
    HALVES = B // HALF
    UR, UD = len(RECT), len(DIAG)
    WJ = BLK * 2 * E
    NG = -(-NPAIR // P)

    def pair(n, m):
        return n * (2 * N - n - 1) // 2 + m - n - 1

    def row_of(half, mb):
        return half * ROWS + ROWS - 1 - mb

    def first_block(half, mb):
        return half * ROWS * (ROWS + 1) // 2 + sum(r + 1 for r in range(mb + 1, ROWS))

    def first_unit(half, mb):
        return sum(first_unit_rows(r) for _ in range(half) for r in range(ROWS)) + sum(
            first_unit_rows(r) for r in range(mb + 1, ROWS))

    def first_unit_rows(r):
        return r * UR + UD

    NK = first_block(HALVES, ROWS - 1)

    tasks, slot_tasks = [], {}

    def add_tasks(place, new):
        for i, t in new:
            slot_tasks.setdefault((place, i), []).append(len(tasks))
            tasks.append(t)

    def x_tasks(xb, half):
        return [("x", xb, half, c, j) for c in range(NC) for j in range(NJ)]

    low = {g: min(m // BLK for n in range(N) for m in range(n + 1, N) if pair(n, m) // P == g) for g in range(NG)}

    def done_groups(half, mb):
        return [(g, half) for g in sorted(low, reverse=True) if low[g] == mb]

    diag_groups = {}
    add_tasks("start", [(0, t) for t in x_tasks(ROWS - 1, 0) + x_tasks(ROWS - 2, 0)])
    for half in range(HALVES):
        if half == 0:
            new = [t for xb in range(ROWS - 3, -1, -1) for t in x_tasks(xb, 0)]
            add_tasks(("first", 0), [(1 + i // 2, t) for i, t in enumerate(new)])
        else:
            add_tasks(("first", half), [(1 + i, t) for i, t in enumerate(x_tasks(0, half))])
        for mb in range(ROWS - 1, -1, -1):
            new = x_tasks(mb + 1, half + 1) if mb + 1 < ROWS and half + 1 < HALVES else []
            groups = done_groups(half, mb + 1) if mb + 1 < ROWS else done_groups(half - 1, 0) if half else []
            diag_groups[half, mb] = groups
            assert len(groups) <= 2
            add_tasks(("diag", half, mb), [(i // 2, t) for i, t in enumerate(new)])
            new = [("out", g, h, c, 0) for g, h in groups for c in range(NC)]
            add_tasks(("diag", half, mb), [(NJ + i * NJ // len(new), t) for i, t in enumerate(new)])
    diag_groups["end"] = done_groups(HALVES - 1, 0)
    add_tasks("end", [(0, ("out", g, h, c, 0)) for g, h in diag_groups["end"] for c in range(NC)])
    task_no = {t: i for i, t in enumerate(tasks)}
    out_order = [(t[1], t[2]) for t in tasks if t[0] == "out" and t[3] == 0]
    x_order = [(t[1], t[2]) for t in tasks if t[0] == "x" and t[3:] == (0, 0)]

    def segments(g):
        runs = []
        for n in range(N):
            a, b = max(pair(n, n + 1), g * P), min(pair(n, n + 1) + N - 1 - n, (g + 1) * P)
            if a < b:
                runs.append((a - g * P, n, n + 1 + a - pair(n, n + 1), b - a))
        return runs

    def width(g):
        return min(P, NPAIR - g * P)

    with ExitStack() as ctx:
        def sb(name, shape, dt=F32):
            return ctx.enter_context(nc.sbuf_tensor(name, shape, dt))

        def sem(name):
            return ctx.enter_context(nc.semaphore(name))

        xT = sb("xT", [P, (N // 2) * HALF])
        stack = sb("stack", [P, BLK, HALF], F32R)
        w_raw = sb("w_raw", [P, 2, WJ])
        w_hi = sb("w_hi", [P, NJ, WJ], F32R)
        w_lo = sb("w_lo", [P, NJ, WJ], F32R)
        x_dup = sb("x_dup", [P, 2, HALF])
        x_nat = sb("x_nat", [P, NC, BANK // P, BLK * E])
        prod = sb("prod", [P, 4, HALF])
        o_blk = sb("o_blk", [P, BANK])
        o_pair = sb("o_pair", [P, 2, HALF])
        o_nat = sb("o_nat", [P, HALF // P, P])
        ident = sb("ident", [P, P])
        pick = sb("pick", [P, 64])

        psT = ctx.enter_context(nc.psum_tensor("psT", [P, 2, NC * BANK], F32))
        psO = ctx.enter_context(nc.psum_tensor("psO", [P, BANK], F32))
        psX = ctx.enter_context(nc.psum_tensor("psX", [P, 2, BANK], F32))
        scratch = nc.dram_tensor("scratch", [N, N, B], F32, kind="Internal").ap()

        const_zero = sem("const_zero")
        const_ready = sem("const_ready")
        x_nat_ready = [sem(f"x_nat_ready{c}") for c in range(NC)]
        turned = sem("turned")
        turn_out = sem("turn_out")
        x_dup_ready = [sem(f"x_dup_ready{i}") for i in range(2)]
        stack_hi_ready = sem("stack_hi_ready")
        stack_ready = sem("stack_ready")
        w_raw_ready = [sem(f"w_raw_ready{i}") for i in range(2)]
        w_hi_ready = sem("w_hi_ready")
        w_ready = sem("w_ready")
        t_ready = sem("t_ready")
        prod_ready = sem("prod_ready")
        sums_ready = sem("sums_ready")
        sums_out = sem("sums_out")
        scratch_ready = sem("scratch_ready")
        o_pair_ready = [sem(f"o_pair_ready{i}") for i in range(2)]
        stored = sem("stored")

        def o_pair_loads(o):
            return 16 * sum(len(segments(out_order[i][0])) for i in range(o % 2, o + 1, 2))

        block = ctx.enter_context(nc.Block())

        def rect_blocks(eng, half, mb):
            k, u, start = first_block(half, mb), first_unit(half, mb), 0
            if mb == ROWS - 1:
                yield k, u, mb - 1, True
                start = 1
            if mb - start == 1:
                yield k + start, u + start * UR, mb - 1 - start, False
            elif mb > start:
                with eng.Fori(start, mb) as i:
                    yield k + i, u + i * UR, i * -1 + (mb - 1), False

        @block.tensor
        def _(pe):
            def turn(t):
                kind, a, half, c, j = tasks[t]
                if t >= 2:
                    pe.wait_ge(turn_out, t - 1)
                if kind == "x":
                    if j == 0:
                        pe.wait_ge(x_nat_ready[c], 16 * (x_order.index((a, half)) + 1))
                    for q in range(4):
                        mm = pe.transpose(psX[:, t % 2, q * P:(q + 1) * P], x_nat[:, c, q, j * P:(j + 1) * P], ident[:, :])
                else:
                    o, n = out_order.index((a, half)), width(a)
                    if c == 0:
                        pe.wait_ge(o_pair_ready[o % 2], o_pair_loads(o))
                    for q in range(4):
                        b0 = c * BANK + q * P
                        mm = pe.transpose(psX[:, t % 2, q * n:(q + 1) * n], o_pair[0:n, o % 2, b0:b0 + P], ident[0:n, 0:n])
                mm.then_inc(turned, 1)

            def sum_group(units, first_pos, seen, last):
                for s in (first_pos, first_pos + 1):
                    j, dm = units[s]
                    for c in range(NC):
                        q = 2 * (dm % 2) + c
                        r = 8 * j + dm // 2
                        mm = pe.matmul(psO[32 * q:32 * q + 32, :], pick[:, 32 - r:64 - r],
                                       prod[:, s % 4, c * BANK:(c + 1) * BANK],
                                       start=q not in seen, stop=last and s == first_pos + 1 or last and dm % 2 == 0)
                        seen.add(q)
                if last:
                    mm.then_inc(sums_ready, 1)

            def one_block(units, k, u, place, stack_count, head):
                seen = set()
                for i in range(len(units) // 2):
                    for s in (2 * i, 2 * i + 1):
                        j, dm = units[s]
                        if all(v[0] != j for v in units[:s]):
                            pe.wait_ge(w_ready, k * NJ + (j + 1))
                        if all(v[1] != dm for v in units[:s]):
                            pe.wait_ge(stack_ready, stack_count + dm + 1)
                        if not (head and s < 2):
                            pe.wait_ge(prod_ready, u + (s - 1))
                        for c in range(NC):
                            t = psT[:, s % 2, c * BANK:(c + 1) * BANK]
                            xs = stack[:, dm, c * BANK:(c + 1) * BANK]
                            pe.matmul(t, w_hi[:, j, dm * P:(dm + 1) * P], xs, start=True, stop=False)
                            mm = pe.matmul(t, w_lo[:, j, dm * P:(dm + 1) * P], xs, start=False, stop=True)
                        mm.then_inc(t_ready, 1)
                    if i > 0:
                        if i == 1 and not head:
                            pe.wait_ge(sums_out, k)
                        sum_group(units, 2 * i - 2, seen, False)
                    elif not head:
                        sum_group(RECT, UR - 2, {0, 1, 2, 3}, True)
                    for t in slot_tasks.get((place, i), []):
                        turn(t)

            pe.wait_ge(const_ready, 4)
            for t in slot_tasks["start", 0]:
                turn(t)
            for half in range(HALVES):
                for mb in range(ROWS - 1, -1, -1):
                    count = BLK * row_of(half, mb)
                    for k, u, nb, peeled in rect_blocks(pe, half, mb):
                        one_block(RECT, k, u, ("first", half) if peeled else None, count, peeled and half == 0)
                    one_block(DIAG, first_block(half, mb) + mb, first_unit(half, mb) + mb * UR,
                              ("diag", half, mb), count, False)
            pe.wait_ge(prod_ready, first_unit(HALVES, ROWS - 1))
            sum_group(RECT, UR - 2, {0, 1, 2, 3}, True)
            for t in slot_tasks["end", 0]:
                turn(t)

        @block.vector
        def _(dve):
            dve.memset(ident[:, :], 0.0).then_inc(const_zero, 1)
            dve.memset(pick[:, :], 0.0).then_inc(const_zero, 1)
            dve.wait_ge(const_zero, 2)
            dve.memset(pick[0:64, 32:33], 1.0).then_inc(const_ready, 1)
            dve.memset(pick[64:128, 36:37], 1.0).then_inc(const_ready, 1)

            def one_block(units, u, nb):
                at = [(nb * NJ + j) * HALF for j in range(NJ)]
                if not isinstance(nb, int):
                    at = [dve.snap(a) for a in at]
                for s, (j, dm) in enumerate(units):
                    dve.wait_ge(t_ready, u + (s + 1))
                    dve.tensor_tensor(prod[:, s % 4, :], psT[:, s % 2, :],
                                      xT[:, bass.ds(at[j], HALF)], ALU.mult).then_inc(prod_ready, 1)

            for half in range(HALVES):
                for mb in range(ROWS - 1, -1, -1):
                    for k, u, nb, peeled in rect_blocks(dve, half, mb):
                        xb = ROWS - 2 if peeled else 0
                        dve.wait_ge(turn_out, task_no["x", xb, half, NC - 1, NJ - 1] + 1)
                        one_block(RECT, u, nb)
                    one_block(DIAG, first_unit(half, mb) + mb * UR, mb)

        END = float("inf")

        def stack_pos(dm):
            return max(last_use(DIAG, 1, d) for d in range(dm + 1))

        def follow(units, place, diag, k, more):
            work = []
            if more:
                work += [(last_use(units, 0, j) + 0.6, "w", j) for j in range(NJ)]
                if diag:
                    work += [(stack_pos(dm) + 0.5, "stack", dm) for dm in range(BLK)]
            work += [(2 * i + 1.8, "turn", t) for (p, i), ts in slot_tasks.items() if p == place and p for t in ts]
            work.append((1.7, "sums", 0))
            return sorted(work)

        @block.scalar
        def _(act):
            def split_w(k, u_free, j):
                act.wait_ge(w_raw_ready[j % 2], (k * 2 + (j // 2 + 1)) * 64)
                if u_free is not None:
                    act.wait_ge(t_ready, u_free)
                act.activation(w_hi[:, j, :].rearrange("p (m a e) -> p m a e", a=2, e=E),
                               w_raw[:, j % 2, :].rearrange("p (a m e) -> p m a e", a=2, e=E),
                               ACT.Copy).then_inc(w_hi_ready, 1)

            def split_x(row, u_free, dm):
                act.wait_ge(x_dup_ready[dm % 2], 32 * (BLK // 2 * row + dm // 2 + 1))
                if u_free is not None:
                    act.wait_ge(t_ready, u_free)
                act.activation(stack[:, dm, :], x_dup[:, dm % 2, :], ACT.Copy).then_inc(stack_hi_ready, 1)

            def take_turned(t):
                kind, a, half, c, j = tasks[t]
                if kind == "x":
                    if half > 0:
                        act.wait_ge(prod_ready, first_unit(half - 1, a) + first_unit_rows(a))
                    dst = xT[:, (a * NJ + j) * HALF + c * BANK:(a * NJ + j) * HALF + (c + 1) * BANK]
                    src = psX[:, t % 2, :]
                else:
                    o, n = out_order.index((a, half)), width(a)
                    if o > 0:
                        act.wait_ge(stored, 16 * o)
                    dst = o_nat[:, 4 * c:4 * c + 4, 0:n]
                    src = psX[:, t % 2, 0:4 * n].rearrange("p (q n) -> p q n", n=n)
                act.wait_ge(turned, t + 1)
                act.activation(dst, src, ACT.Copy).then_inc(turn_out, 1)

            def take_sums(k):
                act.wait_ge(sums_ready, k + 1)
                act.wait_ge(scratch_ready, k * 64)
                act.activation(o_blk[:, :], psO[:, :], ACT.Copy).then_inc(sums_out, 1)

            def one_block(units, k, u, place, diag, row, head=False, more=True):
                for pos, what, i in follow(units, place, diag, k, more):
                    if what == "w":
                        split_w(k + 1, u + (last_use(units, 0, i) + 1), i)
                    elif what == "stack":
                        split_x(row + 1, u + (last_use(units, 1, i) + 1), i)
                    elif what == "turn":
                        take_turned(i)
                    elif not head:
                        if place == ("first", 0):
                            raise AssertionError
                        take_sums(k - 1)

            turns = slot_tasks["start", 0]
            for t in turns[:8]:
                take_turned(t)
            split_w(0, None, 0)
            for t in turns[8:]:
                take_turned(t)
            for dm in range(BLK):
                split_x(0, None, dm)
            for j in range(1, NJ):
                split_w(0, None, j)
            for half in range(HALVES):
                for mb in range(ROWS - 1, -1, -1):
                    row = row_of(half, mb)
                    for k, u, nb, peeled in rect_blocks(act, half, mb):
                        one_block(RECT, k, u, ("first", half) if peeled else None, False, row, head=peeled and half == 0)
                    k = first_block(half, mb) + mb
                    one_block(DIAG, k, first_unit(half, mb) + mb * UR, ("diag", half, mb), True, row, more=k + 1 < NK)
            take_sums(NK - 1)
            for t in slot_tasks["end", 0]:
                take_turned(t)

        @block.gpsimd
        def _(pool):
            pool.wait_ge(const_zero, 2)
            pool.affine_select(out=ident[:, :], in_=ident[:, :], compare_op=ALU.not_equal, fill=1.0, base=0,
                               pattern=[[-1, P]], channel_multiplier=1).then_inc(const_ready, 2)

            def split_w(k, j, stacks_before=None):
                pool.wait_ge(w_hi_ready, k * NJ + (j + 1))
                if stacks_before is not None:
                    pool.wait_ge(stack_ready, stacks_before)
                pool.tensor_tensor(w_lo[:, j, :].rearrange("p (m a e) -> p m a e", a=2, e=E),
                                   w_raw[:, j % 2, :].rearrange("p (a m e) -> p m a e", a=2, e=E),
                                   w_hi[:, j, :].bitcast(F32).rearrange("p (m a e) -> p m a e", a=2, e=E),
                                   ALU.subtract).then_inc(w_ready, 1)

            def split_x(row, dm, slots_before=None):
                pool.wait_ge(stack_hi_ready, BLK * row + dm + 1)
                if slots_before is not None:
                    pool.wait_ge(w_ready, slots_before)
                pool.tensor_tensor(stack[64:128, dm, :], x_dup[64:128, dm % 2, :], stack[64:128, dm, :].bitcast(F32),
                                   ALU.subtract).then_inc(stack_ready, 1)

            def diag_block(k, row):
                before, slots = "w", k * NJ + NJ
                for pos, what, i in follow(DIAG, None, True, k, True):
                    if what == "w":
                        split_w(k + 1, i, BLK * (row + 1) + stacks if before == "stack" else None)
                        slots += 1
                    elif what == "stack":
                        split_x(row + 1, i, slots if before == "w" else None)
                        stacks = i + 1
                    else:
                        continue
                    before = what

            split_w(0, 0)
            for dm in range(BLK):
                split_x(0, dm, 1 if dm == 0 else None)
            for j in range(1, NJ):
                split_w(0, j, BLK if j == 1 else None)
            for half in range(HALVES):
                for mb in range(ROWS - 1, -1, -1):
                    for k, u, nb, peeled in rect_blocks(pool, half, mb):
                        for j in range(NJ):
                            split_w(k + 1, j)
                    k = first_block(half, mb) + mb
                    if k + 1 < NK:
                        diag_block(k, row_of(half, mb))

        @block.sync
        def _(sp):
            blocks = [(half, mb, nb) for half in range(HALVES) for mb in range(ROWS - 1, -1, -1)
                      for nb in list(range(mb - 1, -1, -1)) + [mb]]

            def load_w(k, j):
                half, mb, nb = blocks[k]
                if 4 * k + j >= 2:
                    sp.wait_ge(w_ready, 4 * k + j - 1)
                d0 = 2 * j + 1 if nb == mb else 0
                for a in range(2):
                    i = pair(BLK * nb + 2 * j + a, BLK * mb + d0)
                    for r in range(2):
                        sp.dma_start(w_raw[64 * r:64 * r + 64, j % 2, (a * BLK + d0) * E:(a + 1) * BLK * E],
                                     w[:, i:i + BLK - d0, :].rearrange("f i e -> f (i e)")).then_inc(w_raw_ready[j % 2], 16)

            def load_x(xb, half, c):
                o = x_order.index((xb, half))
                if o > 0:
                    pxb, ph = x_order[o - 1]
                    sp.wait_ge(turned, task_no["x", pxb, ph, c, NJ - 1] + 1)
                b0 = half * HALF + c * BANK
                sp.dma_start(x_nat[:, c, :, :],
                             x[b0:b0 + BANK, BLK * xb:BLK * xb + BLK, :].rearrange("(t p) n e -> p t (n e)", p=P)
                             ).then_inc(x_nat_ready[c], 16)

            def dup_x(row, dm):
                half, mb = row // ROWS, ROWS - 1 - row % ROWS
                if BLK * row + dm >= 2:
                    sp.wait_ge(stack_ready, BLK * row + dm - 1)
                if dm == 0:
                    sp.wait_ge(turn_out, task_no["x", mb, half, NC - 1, NJ - 1] + 1)
                a = dm % 2
                col = (NJ * mb + dm // 2) * HALF
                for r in range(2):
                    sp.dma_start(x_dup[64 * r:64 * r + 64, dm % 2, :],
                                 xT[64 * a:64 * a + 64, col:col + HALF]).then_inc(x_dup_ready[dm % 2], 16)

            def write_sums(k):
                half, mb, nb = blocks[k]
                sp.wait_ge(sums_out, k + 1)
                for q in range(4):
                    a, c = q // 2, q % 2
                    b0 = half * HALF + c * BANK
                    dst = scratch[BLK * nb:BLK * nb + BLK, BLK * mb:BLK * mb + BLK, b0:b0 + BANK]
                    sp.dma_start(dst.rearrange("n (d a) b -> n d a b", a=2)[:, :, a, :],
                                 o_blk[32 * q:32 * q + 32, :]).then_inc(scratch_ready, 16)

            def load_pairs(o, k_last):
                g, half = out_order[o]
                sp.wait_ge(scratch_ready, 64 * (k_last + 1))
                if o >= 2:
                    pg, ph = out_order[o - 2]
                    sp.wait_ge(turned, task_no["out", pg, ph, NC - 1, 0] + 1)
                for p0, n, m, cnt in segments(g):
                    sp.dma_start(o_pair[p0:p0 + cnt, o % 2, :],
                                 scratch[n, m:m + cnt, half * HALF:(half + 1) * HALF]).then_inc(o_pair_ready[o % 2], 16)

            def store(o):
                g, half = out_order[o]
                sp.wait_ge(turn_out, task_no["out", g, half, NC - 1, 0] + 1)
                sp.dma_start(out[half * HALF:(half + 1) * HALF, 0, P * g:P * g + width(g)].rearrange("(t p) i -> p t i", p=P),
                             o_nat[:, :, 0:width(g)]).then_inc(stored, 16)

            load_x(ROWS - 1, 0, 0)
            load_x(ROWS - 1, 0, 1)
            load_w(0, 0)
            load_w(0, 1)
            load_x(ROWS - 2, 0, 0)
            load_x(ROWS - 2, 0, 1)
            xs = iter(x_order[2:])
            dup_x(0, 0)
            dup_x(0, 1)
            for dm in range(2, BLK):
                dup_x(0, dm)
            load_w(0, 2)
            load_w(0, 3)

            for k, (half, mb, nb) in enumerate(blocks):
                diag, peeled = nb == mb, k == first_block(half, ROWS - 1)
                units = DIAG if diag else RECT
                place = ("diag", half, mb) if diag else ("first", half) if peeled else None
                row = row_of(half, mb)
                work = []
                if k + 1 < NK:
                    work += [(-3, "w", 0), (-3, "w", 1)]
                    work += [(last_use(units, 0, j) + 0.65, "w", j + 2) for j in range(2)]
                    if diag:
                        work += [(-2, "dup", 0), (-2, "dup", 1)]
                        work += [(stack_pos(dm) + 0.55, "dup", dm + 2) for dm in range(BLK - 2)]
                if k > 0:
                    work.append((1.75, "sums", k - 1))
                for (p, i), ts in slot_tasks.items():
                    if p == place and p:
                        for t in ts:
                            kind, g, h, c, j = tasks[t]
                            if kind == "out" and c == 1:
                                o = out_order.index((g, h))
                                early = -0.5 if mb > 0 else 1.76
                                work.append((early, "pairs", o))
                                work.append((2 * i + 1.9, "store", o))
                if nb == max(mb - 1, 0) and not diag or mb == 0:
                    if mb + 1 < ROWS and half + 1 < HALVES:
                        work += [(-1, "x", (mb + 1, half + 1, c)) for c in range(NC)]
                if diag and mb == 0 and half + 1 < HALVES:
                    work += [(50, "x", (0, half + 1, c)) for c in range(NC)]
                if k == 0:
                    for xb in range(ROWS - 3, -1, -1):
                        for c in range(NC):
                            before = task_no["x", xb + 1, 0, c, NJ - 1]
                            at = next((i for (p, i), ts in slot_tasks.items() if p == place and before in ts), -1)
                            work.append((2 * at + 1.95, "x", (xb, 0, c)))
                for pos, what, i in sorted(work, key=lambda v: v[0]):
                    if what == "w":
                        load_w(k + 1, i)
                    elif what == "dup":
                        dup_x(row + 1, i)
                    elif what == "sums":
                        write_sums(i)
                    elif what == "pairs":
                        load_pairs(i, k - 2 if pos < 1.75 else k - 1)
                    elif what == "store":
                        store(i)
                    else:
                        load_x(*i)
            write_sums(NK - 1)
            for g, h in diag_groups["end"]:
                load_pairs(out_order.index((g, h)), NK - 1)
            for g, h in diag_groups["end"]:
                store(out_order.index((g, h)))
            sp.wait_ge(stored, 16 * len(out_order))


def kernel(r_inputs, L0_rec_param):
    import numpy as np
    import concourse.bacc as bacc
    from concourse.bass_utils import run_bass_kernel_spmd

    nc = bacc.Bacc("TRN2", target_bir_lowering=False, num_devices=1)
    x = np.ascontiguousarray(r_inputs)
    w = np.ascontiguousarray(L0_rec_param)
    x_ap = nc.dram_tensor("x", x.shape, F32, kind="ExternalInput").ap()
    w_ap = nc.dram_tensor("w", w.shape, F32, kind="ExternalInput").ap()
    out_ap = nc.dram_tensor("out", (x.shape[0], 1, w.shape[1]), F32, kind="ExternalOutput").ap()
    build(nc, x_ap, w_ap, out_ap)
    r = run_bass_kernel_spmd(nc, [{"x": x, "w": w}], core_ids=[0])
    return r.results[0]["out"]
```

```python
from contextlib import ExitStack

import concourse.bass as bass
from concourse import mybir
from concourse.alu_op_type import AluOpType as ALU

F32 = mybir.dt.float32
F32R = mybir.dt.float32r
ACT = mybir.ActivationFunctionType

P = 128
BLK = 8
NJ = BLK // 2
BANK = 512
HALF = 1024
NC = HALF // BANK

LAST = [(2, 6), (3, 7)]
RECT = [(j, d) for j in range(NJ) for d in range(BLK) if (j, d) not in LAST] + LAST
DIAG = [(0, 1), (0, 2), (0, 3), (0, 4), (0, 5), (0, 6), (0, 7), (1, 4), (1, 3), (1, 6), (1, 5), (1, 7),
        (2, 5), (2, 7)] + LAST


def last_use(units, what, value):
    return max([s for s, u in enumerate(units) if u[what] == value], default=-1)


def build(nc, x, w, out):
    B, N, E = x.shape
    NPAIR = w.shape[1]
    assert E * 2 == P and N % BLK == 0 and B % HALF == 0 and NPAIR == N * (N - 1) // 2
    ROWS = N // BLK
    HALVES = B // HALF
    UR, UD = len(RECT), len(DIAG)
    WJ = BLK * 2 * E
    ND = 3
    NG = -(-NPAIR // P)

    def pair(n, m):
        return n * (2 * N - n - 1) // 2 + m - n - 1

    def row_of(half, mb):
        return half * ROWS + ROWS - 1 - mb

    def first_block(half, mb):
        return half * ROWS * (ROWS + 1) // 2 + sum(r + 1 for r in range(mb + 1, ROWS))

    def first_unit(half, mb):
        return sum(first_unit_rows(r) for _ in range(half) for r in range(ROWS)) + sum(
            first_unit_rows(r) for r in range(mb + 1, ROWS))

    def first_unit_rows(r):
        return r * UR + UD

    NK = first_block(HALVES, ROWS - 1)

    tasks, slot_tasks = [], {}

    def add_tasks(place, new):
        for i, t in new:
            slot_tasks.setdefault((place, i), []).append(len(tasks))
            tasks.append(t)

    def x_tasks(xb, half):
        return [("x", xb, half, c, j) for c in range(NC) for j in range(NJ)]

    low = {g: min(m // BLK for n in range(N) for m in range(n + 1, N) if pair(n, m) // P == g) for g in range(NG)}

    def done_groups(half, mb):
        return [(g, half) for g in sorted(low, reverse=True) if low[g] == mb]

    diag_groups = {}
    add_tasks("start", [(0, t) for t in x_tasks(ROWS - 1, 0) + x_tasks(ROWS - 2, 0)])
    for half in range(HALVES):
        if half == 0:
            new = [t for xb in range(ROWS - 3, -1, -1) for t in x_tasks(xb, 0)]
            add_tasks(("first", 0), [(2 + i, t) for i, t in enumerate(new)])
        else:
            add_tasks(("first", half), [(2 * i + 3, t) for i, t in enumerate(x_tasks(0, half))])
        for mb in range(ROWS - 1, -1, -1):
            new = x_tasks(mb + 1, half + 1) if mb + 1 < ROWS and half + 1 < HALVES else []
            groups = done_groups(half, mb + 1) if mb + 1 < ROWS else done_groups(half - 1, 0) if half else []
            diag_groups[half, mb] = groups
            add_tasks(("diag", half, mb), [(i + 1, t) for i, t in enumerate(new)])
            new = [("out", g, h, c, 0) for g, h in groups for c in range(NC)]
            add_tasks(("diag", half, mb), [(10 + i, t) for i, t in enumerate(new)])
    diag_groups["end"] = done_groups(HALVES - 1, 0)
    add_tasks("end", [(0, ("out", g, h, c, 0)) for g, h in diag_groups["end"] for c in range(NC)])
    task_no = {t: i for i, t in enumerate(tasks)}
    out_order = [(t[1], t[2]) for t in tasks if t[0] == "out" and t[3] == 0]
    x_order = [(t[1], t[2]) for t in tasks if t[0] == "x" and t[3:] == (0, 0)]

    def segments(g):
        runs = []
        for n in range(N):
            a, b = max(pair(n, n + 1), g * P), min(pair(n, n + 1) + N - 1 - n, (g + 1) * P)
            if a < b:
                runs.append((a - g * P, n, n + 1 + a - pair(n, n + 1), b - a))
        return runs

    def width(g):
        return min(P, NPAIR - g * P)

    with ExitStack() as ctx:
        def sb(name, shape, dt=F32):
            return ctx.enter_context(nc.sbuf_tensor(name, shape, dt))

        def sem(name):
            return ctx.enter_context(nc.semaphore(name))

        xT = sb("xT", [P, (N // 2) * HALF])
        stack = sb("stack", [P, BLK, HALF], F32R)
        w_raw = sb("w_raw", [P, 2, WJ])
        w_hi = sb("w_hi", [P, NJ, WJ], F32R)
        w_lo = sb("w_lo", [P, NJ, WJ], F32R)
        x_dup = sb("x_dup", [P, ND, HALF])
        x_nat = sb("x_nat", [P, NC, BANK // P, BLK * E])
        prod = sb("prod", [P, 4, HALF])
        o_blk = sb("o_blk", [P, BANK])
        o_pair = sb("o_pair", [P, HALF])
        o_nat = sb("o_nat", [P, HALF // P, P])
        ident = sb("ident", [P, P])
        pick = sb("pick", [P, 64])

        psT = ctx.enter_context(nc.psum_tensor("psT", [P, 3, NC * BANK], F32))
        psO = ctx.enter_context(nc.psum_tensor("psO", [P, BANK], F32))
        psX = ctx.enter_context(nc.psum_tensor("psX", [P, BANK], F32))

        N_START = len(slot_tasks["start", 0])

        def turn_bank(t):
            return psT[:, t % 6 // 2, t % 2 * BANK:(t % 2 + 1) * BANK] if t < N_START else psX[:, :]

        def turn_before(t):
            return t - 6 if t < N_START else t - 1 if t > N_START else -1

        scratch = nc.dram_tensor("scratch", [N, N, B], F32, kind="Internal").ap()

        const_zero = sem("const_zero")
        const_ready = sem("const_ready")
        x_nat_ready = [sem(f"x_nat_ready{c}") for c in range(NC)]
        turned = sem("turned")
        turn_out = sem("turn_out")
        x_dup_ready = [sem(f"x_dup_ready{i}") for i in range(ND)]
        stack_hi_ready = sem("stack_hi_ready")
        stack_ready = sem("stack_ready")
        w_raw_ready = [sem(f"w_raw_ready{i}") for i in range(2)]
        w_hi_ready = sem("w_hi_ready")
        w_ready = sem("w_ready")
        t_ready = sem("t_ready")
        prod_ready = sem("prod_ready")
        sums_ready = sem("sums_ready")
        sums_out = sem("sums_out")
        scratch_ready = sem("scratch_ready")
        o_pair_ready = sem("o_pair_ready")
        stored = sem("stored")

        def o_pair_loads(o):
            return 16 * sum(len(segments(out_order[i][0])) for i in range(o + 1))

        block = ctx.enter_context(nc.Block())

        def rect_blocks(eng, half, mb):
            k, u, start = first_block(half, mb), first_unit(half, mb), 0
            if mb == ROWS - 1:
                yield k, u, mb - 1, True
                start = 1
            if mb - start == 1:
                yield k + start, u + start * UR, mb - 1 - start, False
            elif mb > start:
                with eng.Fori(start, mb) as i:
                    yield k + i, u + i * UR, i * -1 + (mb - 1), False

        rect_slots = [s % 3 for s in range(UR)]
        diag_slots = {True: [(s + 2) % 3 for s in range(UD)], False: [s % 3 for s in range(UD)]}

        def tail(slots):
            return {v: max(s for s in range(len(slots)) if slots[s] == v) - len(slots) for v in range(3)}

        either_tail = {v: max(tail(rect_slots)[v], tail(diag_slots[True])[v]) for v in range(3)}

        @block.tensor
        def _(pe):
            def turn(t):
                kind, a, half, c, j = tasks[t]
                if turn_before(t) >= 0:
                    pe.wait_ge(turn_out, turn_before(t) + 1)
                if kind == "x":
                    if j == 0:
                        pe.wait_ge(x_nat_ready[c], 16 * (x_order.index((a, half)) + 1))
                    for q in range(4):
                        mm = pe.transpose(turn_bank(t)[:, q * P:(q + 1) * P], x_nat[:, c, q, j * P:(j + 1) * P], ident[:, :])
                else:
                    o, n = out_order.index((a, half)), width(a)
                    if c == 0:
                        pe.wait_ge(o_pair_ready, o_pair_loads(o))
                    for q in range(4):
                        b0 = c * BANK + q * P
                        mm = pe.transpose(turn_bank(t)[:, q * n:(q + 1) * n], o_pair[0:n, b0:b0 + P], ident[0:n, 0:n])
                mm.then_inc(turned, 1)

            def sum_group(units, first_pos, seen, last):
                for s in (first_pos, first_pos + 1):
                    j, dm = units[s]
                    for c in range(NC):
                        q = 2 * (dm % 2) + c
                        r = 8 * j + dm // 2
                        mm = pe.matmul(psO[32 * q:32 * q + 32, :], pick[:, 32 - r:64 - r],
                                       prod[:, s % 4, c * BANK:(c + 1) * BANK],
                                       start=q not in seen, stop=last and s == first_pos + 1 or last and dm % 2 == 0)
                        seen.add(q)
                if last:
                    mm.then_inc(sums_ready, 1)

            def one_block(units, k, u, slots, before, place, stack_count, head):
                seen = set()
                for s, (j, dm) in enumerate(units):
                    if all(v[0] != j for v in units[:s]):
                        pe.wait_ge(w_ready, k * NJ + (j + 1))
                    if all(v[1] != dm for v in units[:s]):
                        pe.wait_ge(stack_ready, stack_count + dm + 1)
                    last = max([v for v in range(s) if slots[v] == slots[s]], default=None)
                    if last is None and before is not None:
                        last = before[slots[s]]
                    if last is not None:
                        pe.wait_ge(prod_ready, u + (last + 1))
                    elif s < 3:
                        pe.wait_ge(turn_out, N_START)
                    for c in range(NC):
                        t = psT[:, slots[s], c * BANK:(c + 1) * BANK]
                        xs = stack[:, dm, c * BANK:(c + 1) * BANK]
                        pe.matmul(t, w_hi[:, j, dm * P:(dm + 1) * P], xs, start=True, stop=False)
                        mm = pe.matmul(t, w_lo[:, j, dm * P:(dm + 1) * P], xs, start=False, stop=True)
                    mm.then_inc(t_ready, 1)
                    if s % 2 == 1:
                        if s > 1:
                            pe.wait_ge(prod_ready, u + (s - 1))
                            if s == 3 and not head:
                                pe.wait_ge(sums_out, k)
                            sum_group(units, s - 3, seen, False)
                        elif not head:
                            pe.wait_ge(prod_ready, u)
                            sum_group(RECT, UR - 2, {0, 1, 2, 3}, True)
                    for t in slot_tasks.get((place, s), []):
                        turn(t)

            pe.wait_ge(const_ready, 4)
            for t in slot_tasks["start", 0]:
                turn(t)
            for half in range(HALVES):
                for mb in range(ROWS - 1, -1, -1):
                    count = BLK * row_of(half, mb)
                    for k, u, nb, peeled in rect_blocks(pe, half, mb):
                        head = peeled and half == 0
                        before = None if head else tail(diag_slots[False]) if peeled else either_tail
                        one_block(RECT, k, u, rect_slots, before, ("first", half) if peeled else None, count, head)
                    one_block(DIAG, first_block(half, mb) + mb, first_unit(half, mb) + mb * UR, diag_slots[mb > 0],
                              tail(rect_slots if mb > 0 else diag_slots[True]), ("diag", half, mb), count, False)
            pe.wait_ge(prod_ready, first_unit(HALVES, ROWS - 1))
            sum_group(RECT, UR - 2, {0, 1, 2, 3}, True)
            for t in slot_tasks["end", 0]:
                turn(t)

        @block.vector
        def _(dve):
            dve.memset(ident[:, :], 0.0).then_inc(const_zero, 1)
            dve.memset(pick[:, :], 0.0).then_inc(const_zero, 1)
            dve.wait_ge(const_zero, 2)
            dve.memset(pick[0:64, 32:33], 1.0).then_inc(const_ready, 1)
            dve.memset(pick[64:128, 36:37], 1.0).then_inc(const_ready, 1)

            def one_block(units, slots, u, nb):
                at = [(nb * NJ + j) * HALF for j in range(NJ)]
                if not isinstance(nb, int):
                    at = [dve.snap(a) for a in at]
                for s, (j, dm) in enumerate(units):
                    dve.wait_ge(t_ready, u + (s + 1))
                    dve.tensor_tensor(prod[:, s % 4, :], psT[:, slots[s], :],
                                      xT[:, bass.ds(at[j], HALF)], ALU.mult).then_inc(prod_ready, 1)

            for dm in range(BLK):
                dve.wait_ge(stack_hi_ready, dm + 1)
                dve.tensor_tensor(stack[64:128, dm, :], x_dup[64:128, dm % ND, :], stack[64:128, dm, :].bitcast(F32),
                                  ALU.subtract).then_inc(stack_ready, 1)

            for half in range(HALVES):
                for mb in range(ROWS - 1, -1, -1):
                    for k, u, nb, peeled in rect_blocks(dve, half, mb):
                        xb = ROWS - 2 if peeled else 0
                        dve.wait_ge(turn_out, task_no["x", xb, half, NC - 1, NJ - 1] + 1)
                        one_block(RECT, rect_slots, u, nb)
                    one_block(DIAG, diag_slots[mb > 0], first_unit(half, mb) + mb * UR, mb)

        END = float("inf")

        def stack_pos(dm):
            return max([last_use(DIAG, 1, d) for d in range(dm + 1)] + [2 * dm - 2])

        def follow(units, place, diag, k, more):
            work = []
            if more:
                work += [(last_use(units, 0, j) + 0.6, "w", j) for j in range(NJ)]
                if diag:
                    work += [(stack_pos(dm) + 0.5, "stack", dm) for dm in range(BLK)]
            work += [(i + 0.8, "turn", t) for (p, i), ts in slot_tasks.items() if p == place and p for t in ts]
            work.append((1.7, "sums", 0))
            return sorted(work)

        @block.scalar
        def _(act):
            def split_w(k, u_free, j):
                act.wait_ge(w_raw_ready[j % 2], (k * 2 + (j // 2 + 1)) * 64)
                if u_free is not None:
                    act.wait_ge(t_ready, u_free)
                act.activation(w_hi[:, j, :].rearrange("p (m a e) -> p m a e", a=2, e=E),
                               w_raw[:, j % 2, :].rearrange("p (a m e) -> p m a e", a=2, e=E),
                               ACT.Copy).then_inc(w_hi_ready, 1)

            def split_x(row, u_free, dm):
                i = BLK * row + dm
                act.wait_ge(x_dup_ready[i % ND], 32 * (i // ND + 1))
                if u_free is not None:
                    act.wait_ge(t_ready, u_free)
                act.activation(stack[:, dm, :], x_dup[:, i % ND, :], ACT.Copy).then_inc(stack_hi_ready, 1)

            def take_turned(t):
                kind, a, half, c, j = tasks[t]
                if kind == "x":
                    if half > 0:
                        act.wait_ge(prod_ready, first_unit(half - 1, a) + first_unit_rows(a))
                    dst = xT[:, (a * NJ + j) * HALF + c * BANK:(a * NJ + j) * HALF + (c + 1) * BANK]
                    src = turn_bank(t)
                else:
                    o, n = out_order.index((a, half)), width(a)
                    if o > 0:
                        act.wait_ge(stored, 16 * o)
                    dst = o_nat[:, 4 * c:4 * c + 4, 0:n]
                    src = turn_bank(t)[:, 0:4 * n].rearrange("p (q n) -> p q n", n=n)
                act.wait_ge(turned, t + 1)
                act.activation(dst, src, ACT.Copy).then_inc(turn_out, 1)

            def take_sums(k):
                act.wait_ge(sums_ready, k + 1)
                act.wait_ge(scratch_ready, k * 64)
                act.activation(o_blk[:, :], psO[:, :], ACT.Copy).then_inc(sums_out, 1)

            def one_block(units, k, u, place, diag, row, head=False, more=True):
                for pos, what, i in follow(units, place, diag, k, more):
                    if what == "w":
                        split_w(k + 1, u + (last_use(units, 0, i) + 1), i)
                    elif what == "stack":
                        split_x(row + 1, u + (last_use(units, 1, i) + 1), i)
                    elif what == "turn":
                        take_turned(i)
                    elif not head:
                        if place == ("first", 0):
                            raise AssertionError
                        take_sums(k - 1)

            turns = slot_tasks["start", 0]
            for t in turns[:8]:
                take_turned(t)
            split_w(0, None, 0)
            for t in turns[8:]:
                take_turned(t)
            for dm in range(BLK):
                split_x(0, None, dm)
            for j in range(1, NJ):
                split_w(0, None, j)
            for half in range(HALVES):
                for mb in range(ROWS - 1, -1, -1):
                    row = row_of(half, mb)
                    for k, u, nb, peeled in rect_blocks(act, half, mb):
                        one_block(RECT, k, u, ("first", half) if peeled else None, False, row, head=peeled and half == 0)
                    k = first_block(half, mb) + mb
                    one_block(DIAG, k, first_unit(half, mb) + mb * UR, ("diag", half, mb), True, row, more=k + 1 < NK)
            take_sums(NK - 1)
            for t in slot_tasks["end", 0]:
                take_turned(t)

        @block.gpsimd
        def _(pool):
            pool.wait_ge(const_zero, 2)
            pool.affine_select(out=ident[:, :], in_=ident[:, :], compare_op=ALU.not_equal, fill=1.0, base=0,
                               pattern=[[-1, P]], channel_multiplier=1).then_inc(const_ready, 2)

            def split_w(k, j, stacks_before=None):
                pool.wait_ge(w_hi_ready, k * NJ + (j + 1))
                if stacks_before is not None:
                    pool.wait_ge(stack_ready, stacks_before)
                pool.tensor_tensor(w_lo[:, j, :].rearrange("p (m a e) -> p m a e", a=2, e=E),
                                   w_raw[:, j % 2, :].rearrange("p (a m e) -> p m a e", a=2, e=E),
                                   w_hi[:, j, :].bitcast(F32).rearrange("p (m a e) -> p m a e", a=2, e=E),
                                   ALU.subtract).then_inc(w_ready, 1)

            def split_x(row, dm, slots_before=None):
                pool.wait_ge(stack_hi_ready, BLK * row + dm + 1)
                if slots_before is not None:
                    pool.wait_ge(w_ready, slots_before)
                pool.tensor_tensor(stack[64:128, dm, :], x_dup[64:128, (BLK * row + dm) % ND, :], stack[64:128, dm, :].bitcast(F32),
                                   ALU.subtract).then_inc(stack_ready, 1)

            def diag_block(k, row):
                before, slots = "w", k * NJ + NJ
                for pos, what, i in follow(DIAG, None, True, k, True):
                    if what == "w":
                        split_w(k + 1, i, BLK * (row + 1) + stacks if before == "stack" else None)
                        slots += 1
                    elif what == "stack":
                        split_x(row + 1, i, slots if before == "w" else None)
                        stacks = i + 1
                    else:
                        continue
                    before = what

            for j in range(NJ):
                split_w(0, j)
            for half in range(HALVES):
                for mb in range(ROWS - 1, -1, -1):
                    for k, u, nb, peeled in rect_blocks(pool, half, mb):
                        for j in range(NJ):
                            split_w(k + 1, j)
                    k = first_block(half, mb) + mb
                    if k + 1 < NK:
                        diag_block(k, row_of(half, mb))

        @block.sync
        def _(sp):
            blocks = [(half, mb, nb) for half in range(HALVES) for mb in range(ROWS - 1, -1, -1)
                      for nb in list(range(mb - 1, -1, -1)) + [mb]]

            def load_w(k, j):
                half, mb, nb = blocks[k]
                if 4 * k + j >= 2:
                    sp.wait_ge(w_ready, 4 * k + j - 1)
                d0 = 2 * j + 1 if nb == mb else 0
                for a in range(2):
                    i = pair(BLK * nb + 2 * j + a, BLK * mb + d0)
                    for r in range(2):
                        sp.dma_start(w_raw[64 * r:64 * r + 64, j % 2, (a * BLK + d0) * E:(a + 1) * BLK * E],
                                     w[:, i:i + BLK - d0, :].rearrange("f i e -> f (i e)")).then_inc(w_raw_ready[j % 2], 16)

            def load_x(xb, half, c):
                o = x_order.index((xb, half))
                if o > 0:
                    pxb, ph = x_order[o - 1]
                    sp.wait_ge(turned, task_no["x", pxb, ph, c, NJ - 1] + 1)
                b0 = half * HALF + c * BANK
                sp.dma_start(x_nat[:, c, :, :],
                             x[b0:b0 + BANK, BLK * xb:BLK * xb + BLK, :].rearrange("(t p) n e -> p t (n e)", p=P)
                             ).then_inc(x_nat_ready[c], 16)

            def dup_x(row, dm):
                half, mb = row // ROWS, ROWS - 1 - row % ROWS
                i = BLK * row + dm
                if i >= ND:
                    sp.wait_ge(stack_ready, i - ND + 1)
                if dm == 0:
                    sp.wait_ge(turn_out, task_no["x", mb, half, NC - 1, NJ - 1] + 1)
                a = dm % 2
                col = (NJ * mb + dm // 2) * HALF
                for r in range(2):
                    sp.dma_start(x_dup[64 * r:64 * r + 64, i % ND, :],
                                 xT[64 * a:64 * a + 64, col:col + HALF]).then_inc(x_dup_ready[i % ND], 16)

            def write_sums(k):
                half, mb, nb = blocks[k]
                sp.wait_ge(sums_out, k + 1)
                for q in range(4):
                    a, c = q // 2, q % 2
                    b0 = half * HALF + c * BANK
                    dst = scratch[BLK * nb:BLK * nb + BLK, BLK * mb:BLK * mb + BLK, b0:b0 + BANK]
                    sp.dma_start(dst.rearrange("n (d a) b -> n d a b", a=2)[:, :, a, :],
                                 o_blk[32 * q:32 * q + 32, :]).then_inc(scratch_ready, 16)

            def load_pairs(o, k_last):
                g, half = out_order[o]
                sp.wait_ge(scratch_ready, 64 * (k_last + 1))
                if o >= 1:
                    pg, ph = out_order[o - 1]
                    sp.wait_ge(turned, task_no["out", pg, ph, NC - 1, 0] + 1)
                for p0, n, m, cnt in segments(g):
                    sp.dma_start(o_pair[p0:p0 + cnt, :],
                                 scratch[n, m:m + cnt, half * HALF:(half + 1) * HALF]).then_inc(o_pair_ready, 16)

            def store(o):
                g, half = out_order[o]
                sp.wait_ge(turn_out, task_no["out", g, half, NC - 1, 0] + 1)
                sp.dma_start(out[half * HALF:(half + 1) * HALF, 0, P * g:P * g + width(g)].rearrange("(t p) i -> p t i", p=P),
                             o_nat[:, :, 0:width(g)]).then_inc(stored, 16)

            load_x(ROWS - 1, 0, 0)
            load_x(ROWS - 1, 0, 1)
            load_w(0, 0)
            load_w(0, 1)
            load_x(ROWS - 2, 0, 0)
            dup_x(0, 0)
            dup_x(0, 1)
            load_x(ROWS - 2, 0, 1)
            for dm in range(2, BLK):
                dup_x(0, dm)
            load_w(0, 2)
            load_w(0, 3)

            for k, (half, mb, nb) in enumerate(blocks):
                diag, peeled = nb == mb, k == first_block(half, ROWS - 1)
                units = DIAG if diag else RECT
                place = ("diag", half, mb) if diag else ("first", half) if peeled else None
                row = row_of(half, mb)
                work = []
                if k + 1 < NK:
                    work += [(-3, "w", 0), (-3, "w", 1)]
                    work += [(last_use(units, 0, j) + 0.65, "w", j + 2) for j in range(2)]
                    if diag:
                        work += [(stack_pos(dm) + 0.55, "dup", dm + ND) for dm in range(BLK - ND)]
                    if nb == 0:
                        work += [(-2, "dup", dm) for dm in range(ND)]
                if k > 0:
                    work.append((1.75, "sums", k - 1))
                for (p, i), ts in slot_tasks.items():
                    if p == place and p:
                        for t in ts:
                            kind, g, h, c, j = tasks[t]
                            if kind == "out" and c == 1:
                                o = out_order.index((g, h))
                                early = -0.5 if mb > 0 else 1.76
                                if diag_groups[half, mb].index((g, h)) > 0:
                                    early = i - 1.1
                                work.append((early, "pairs", o))
                                work.append((i + 0.9, "store", o))
                if half + 1 < HALVES:
                    if k == first_block(half, ROWS - 1) + 1:
                        work += [(-1, "x", (ROWS - 1, half + 1, c)) for c in range(NC)]
                    if diag and mb < ROWS - 1:
                        work += [(NJ * (c + 1) + 0.9, "x", (mb, half + 1, c)) for c in range(NC)]
                if k == 0:
                    for xb in range(ROWS - 3, -1, -1):
                        for c in range(NC):
                            before = task_no["x", xb + 1, 0, c, NJ - 1]
                            at = next((i for (p, i), ts in slot_tasks.items() if p == place and before in ts), -1)
                            work.append((at + 0.9, "x", (xb, 0, c)))
                for pos, what, i in sorted(work, key=lambda v: v[0]):
                    if what == "w":
                        load_w(k + 1, i)
                    elif what == "dup":
                        dup_x(row + 1, i)
                    elif what == "sums":
                        write_sums(i)
                    elif what == "pairs":
                        load_pairs(i, k - 2 if pos < 1.75 else k - 1)
                    elif what == "store":
                        store(i)
                    else:
                        load_x(*i)
            write_sums(NK - 1)
            for g, h in diag_groups["end"]:
                load_pairs(out_order.index((g, h)), NK - 1)
            for g, h in diag_groups["end"]:
                store(out_order.index((g, h)))
            sp.wait_ge(stored, 16 * len(out_order))


def kernel(r_inputs, L0_rec_param):
    import numpy as np
    import concourse.bacc as bacc
    from concourse.bass_utils import run_bass_kernel_spmd

    nc = bacc.Bacc("TRN2", target_bir_lowering=False, num_devices=1)
    x = np.ascontiguousarray(r_inputs)
    w = np.ascontiguousarray(L0_rec_param)
    x_ap = nc.dram_tensor("x", x.shape, F32, kind="ExternalInput").ap()
    w_ap = nc.dram_tensor("w", w.shape, F32, kind="ExternalInput").ap()
    out_ap = nc.dram_tensor("out", (x.shape[0], 1, w.shape[1]), F32, kind="ExternalOutput").ap()
    build(nc, x_ap, w_ap, out_ap)
    r = run_bass_kernel_spmd(nc, [{"x": x, "w": w}], core_ids=[0])
    return r.results[0]["out"]
```

```python
from contextlib import ExitStack

import concourse.bass as bass
from concourse import mybir
from concourse.alu_op_type import AluOpType as ALU

F32 = mybir.dt.float32
F32R = mybir.dt.float32r
ACT = mybir.ActivationFunctionType

P = 128
BLK = 8
NJ = BLK // 2
BANK = 512
HALF = 1024
NC = HALF // BANK

LAST = [(2, 6), (3, 7)]
RECT = ([(j, d) for j in range(NJ) for d in range(2)]
        + [(j, d) for j in range(NJ) for d in range(2, BLK) if (j, d) not in LAST] + LAST)
DIAG = [(0, 1), (0, 3), (0, 2), (0, 4), (0, 5), (0, 7), (0, 6), (1, 4), (1, 3), (1, 5), (1, 6), (1, 7),
        (2, 5), (2, 7)] + LAST


def members(diag, side, h):
    if not diag:
        return slice(4 * h + side, 4 * h + 4, 2)
    return slice(4 * h, 4 * h + 4, 3) if side else slice(4 * h + 1, 4 * h + 3)


def sum_place(diag, dm):
    return next((side, 16 * h + two.index(dm)) for side in range(2) for h in range(2)
                for two in [list(range(BLK))[members(diag, side, h)]] if dm in two)


for units, diag in ((RECT, False), (DIAG, True)):
    assert all(sum_place(diag, units[i][1])[0] != sum_place(diag, units[i + 1][1])[0] for i in range(0, len(units), 2))
assert all(sum_place(False, dm) == sum_place(True, dm) for _, dm in LAST)


def last_use(units, what, value):
    return max([s for s, u in enumerate(units) if u[what] == value], default=-1)


def build(nc, x, w, out):
    B, N, E = x.shape
    NPAIR = w.shape[1]
    assert E * 2 == P and N % BLK == 0 and B % HALF == 0 and NPAIR == N * (N - 1) // 2
    ROWS = N // BLK
    HALVES = B // HALF
    WJ = BLK * 2 * E
    ND = 3
    NG = -(-NPAIR // P)

    def pair(n, m):
        return n * (2 * N - n - 1) // 2 + m - n - 1

    FIRST_X = 7

    UR, UD = len(RECT), len(DIAG)

    def row_of(half, mb):
        return half * ROWS + ROWS - 1 - mb

    def first_block(half, mb):
        return half * ROWS * (ROWS + 1) // 2 + sum(r + 1 for r in range(mb + 1, ROWS))

    def first_unit(half, mb):
        return sum(first_unit_rows(r) for _ in range(half) for r in range(ROWS)) + sum(
            first_unit_rows(r) for r in range(mb + 1, ROWS))

    def first_unit_rows(r):
        return r * UR + UD

    NK = first_block(HALVES, ROWS - 1)

    tasks, slot_tasks = [], {}

    def add_tasks(place, new):
        for i, t in new:
            slot_tasks.setdefault((place, i), []).append(len(tasks))
            tasks.append(t)

    def x_tasks(xb, half):
        return [("x", xb, half, c, j) for c in range(NC) for j in range(NJ)]

    low = {g: min(m // BLK for n in range(N) for m in range(n + 1, N) if pair(n, m) // P == g) for g in range(NG)}

    def done_groups(half, mb):
        return [(g, half) for g in sorted(low, reverse=True) if low[g] == mb]

    end_groups = done_groups(HALVES - 1, 0)
    late_pairs = [(n, m) for n in range(BLK) for m in range(n + 1, BLK)]
    NL = len(late_pairs)

    xn = [("x", ROWS - 2, 0, c, j) for j0 in range(0, NJ, 2) for c in range(NC) for j in (j0, j0 + 1)]
    add_tasks("start", [(0, t) for t in x_tasks(ROWS - 1, 0) + xn[:2 * NC]])
    add_tasks(("first", 0), [(2 + i, t) for i, t in enumerate(sorted(xn[2 * NC:], key=lambda t: t[4]))])
    for half in range(HALVES):
        new = [t for xb in (range(ROWS - 3, -1, -1) if half == 0 else [0]) for t in x_tasks(xb, half)]
        add_tasks(("first", half), [((FIRST_X + i * (UR - 1 - FIRST_X) // (len(new) - 1)) if half == 0 else 2 + i, t)
                                    for i, t in enumerate(new)])
        done = done_groups(half - 1, 1) + done_groups(half - 1, 0) if half else []
        for at, (g, h) in zip((15, UR - 3), done):
            add_tasks(("first", half), [(at + c, ("out", g, h, c, 0)) for c in range(NC)])
        for mb in range(ROWS - 1, -1, -1):
            new = x_tasks(mb + 1, half + 1) if mb + 1 < ROWS and half + 1 < HALVES else []
            add_tasks(("diag", half, mb), [(i + (1 if mb else 4), t) for i, t in enumerate(new)])
            if mb == ROWS - 1:
                groups = done[2:]
            elif mb > 0:
                groups = done_groups(half, mb + 1)
            else:
                groups = end_groups + done_groups(half, 1) if half == HALVES - 1 else []
            places = (UD - 5,) if len(groups) < 2 else (2, UD - 3) if mb else range(UD - 2 * len(groups), UD, 2)
            for at, (g, h) in zip(places, groups):
                add_tasks(("diag", half, mb), [(at + c, ("out", g, h, c, 0)) for c in range(NC)])
    assert sorted(t[1:3] for t in tasks if t[0] == "out" and t[3]) == [(g, h) for g in range(NG) for h in range(HALVES)]
    task_no = {t: i for i, t in enumerate(tasks)}
    out_order = [(t[1], t[2]) for t in tasks if t[0] == "out" and t[3] == 0]
    x_order = [(t[1], t[2]) for t in tasks if t[0] == "x" and t[3:] == (0, 0)]
    XP = NJ // 2

    def segments(g):
        runs = []
        for n in range(N):
            a, b = max(pair(n, n + 1), g * P), min(pair(n, n + 1) + N - 1 - n, (g + 1) * P)
            if a < b:
                runs.append((a - g * P, n, n + 1 + a - pair(n, n + 1), b - a))
        return runs

    def width(g):
        return min(P, NPAIR - g * P)

    with ExitStack() as ctx:
        def sb(name, shape, dt=F32):
            return ctx.enter_context(nc.sbuf_tensor(name, shape, dt))

        def sem(name):
            return ctx.enter_context(nc.semaphore(name))

        xT = sb("xT", [P, (N // 2) * HALF])
        stack = sb("stack", [P, BLK, HALF], F32R)
        w_raw = sb("w_raw", [P, 2, WJ])
        w_hi = sb("w_hi", [P, NJ, WJ], F32R)
        w_lo = sb("w_lo", [P, NJ, WJ], F32R)
        x_part = sb("x_part", [P, ND, HALF], F32R)
        x_nat = sb("x_nat", [P, NC, BANK // P, BLK * E])
        prod = sb("prod", [P, 4, HALF])
        o_blk = sb("o_blk", [P, BANK])
        o_pair = sb("o_pair", [P, HALF])
        o_nat = sb("o_nat", [P, HALF // P, P])
        ident = sb("ident", [P, P])
        late_pick = sb("late_pick", [P, NC, NL])
        pick = sb("pick", [P, 64])

        psT = ctx.enter_context(nc.psum_tensor("psT", [P, 3, NC * BANK], F32))
        psO = ctx.enter_context(nc.psum_tensor("psO", [P, BANK], F32))
        psX = ctx.enter_context(nc.psum_tensor("psX", [P, BANK], F32))

        N_START = len(slot_tasks["start", 0])

        def turn_bank(t):
            return psT[:, t % 6 // 2, t % 2 * BANK:(t % 2 + 1) * BANK] if t < N_START else psX[:, :]

        def turn_before(t):
            return t - 6 if t < N_START else t - 1 if t > N_START else -1

        def late_bank(t):
            return psT[:, t // 2, t % 2 * BANK:t % 2 * BANK + NC * NL]

        scratch = nc.dram_tensor("scratch", [N, N, B], F32, kind="Internal").ap()

        const_zero = sem("const_zero")
        const_ready = sem("const_ready")
        x_nat_ready = [[sem(f"x_nat_ready{c}_{part}") for part in range(NJ // XP)] for c in range(NC)]
        turned = sem("turned")
        turn_out = sem("turn_out")
        x_hi_ready = sem("x_hi_ready")
        x_lo_ready = sem("x_lo_ready")
        stack_hi_ready = [sem(f"stack_hi_ready{dm}") for dm in range(BLK)]
        stack_lo_ready = [sem(f"stack_lo_ready{dm}") for dm in range(BLK)]
        w_raw_ready = [sem(f"w_raw_ready{i}") for i in range(2)]
        w_hi_ready = sem("w_hi_ready")
        w_ready = sem("w_ready")
        t_ready = sem("t_ready")
        prod_ready = sem("prod_ready")
        sums_ready = sem("sums_ready")
        sums_out = sem("sums_out")
        scratch_ready = sem("scratch_ready")
        o_pair_ready = [sem(f"o_pair_ready{i}") for i in range(1 + len(end_groups) + len(done_groups(HALVES - 1, 1)))]
        late_pick_ready = sem("late_pick_ready")
        late_ready = sem("late_ready")
        late_act = sem("late_act")
        late_dve = sem("late_dve")
        stored = sem("stored")

        N_XT = len(end_groups) + len(done_groups(HALVES - 1, 1))

        def in_xT(i):
            return xT[:, (N // 2 - 1 - i) * HALF:(N // 2 - i) * HALF]

        def pair_slot(o):
            i = o - (len(out_order) - N_XT)
            return (o_pair[:, :], o_pair_ready[0]) if i < 0 else (in_xT(i), o_pair_ready[i + 1])

        def nat_slot(o):
            i = o - (len(out_order) - N_XT)
            return o_nat[:, :, :] if i < 0 else in_xT(N_XT + i).rearrange("p (t i) -> p t i", i=P)

        def parts_of(o):
            if out_order[o] not in end_groups:
                return segments(out_order[o][0])
            cut = [(p + max(0, BLK - m), n, max(m, BLK), m + cnt - max(m, BLK)) for p, n, m, cnt in segments(out_order[o][0])]
            return [v for v in cut if v[3] > 0]

        def late_runs(g):
            return [(p, late_pairs.index((n, m)), min(BLK - m, cnt)) for p, n, m, cnt in segments(g) if m < BLK]

        def put_late(tiles, copy, done):
            for g, h in end_groups:
                for p, i, cnt in late_runs(g):
                    dst = nat_slot(out_order.index((g, h)))[:, :, p:p + cnt].rearrange("p (c t) i -> p c t i", c=NC)
                    for t in tiles:
                        copy(dst[:, :, t, :], late_bank(t).rearrange("p (c i) -> p c i", c=NC)[:, :, i:i + cnt]).then_inc(done, 1)

        def o_pair_loads(o):
            mine = range(o + 1) if o < len(out_order) - N_XT else [o]
            return 16 * sum(len(parts_of(i)) for i in mine)

        NITEM = 2 * (BLK // 2)

        def part(row, item):
            return x_part[:, (NITEM * row + item) % ND, :]

        def wait_part_free(eng, row, item):
            r, i = divmod(NITEM * row + item - ND, NITEM)
            if r >= 0:
                for dm in (i // 2 * 2, i // 2 * 2 + 1):
                    eng.wait_ge((stack_lo_ready if i % 2 else stack_hi_ready)[dm], 16 * (r + 1))
                if i % 2 == 0:
                    eng.wait_ge(x_lo_ready, BLK // 2 * r + i // 2 + 1)

        def x_pair(half, mb, p):
            return xT[:, (NJ * mb + p) * HALF:(NJ * mb + p + 1) * HALF]

        block = ctx.enter_context(nc.Block())

        def rect_blocks(eng, half, mb):
            k, u, start = first_block(half, mb), first_unit(half, mb), 0
            if mb == ROWS - 1:
                yield k, u, mb - 1, True
                start = 1
            if mb - start == 1:
                yield k + start, u + start * UR, mb - 1 - start, False
            elif mb > start:
                with eng.Fori(start, mb) as i:
                    yield k + i, u + i * UR, i * -1 + (mb - 1), False

        rect_slots = [s % 3 for s in range(UR)]
        diag_slots = {True: [(s + 2) % 3 for s in range(UD)], False: [s % 3 for s in range(UD)]}

        def tail(slots):
            return {v: max(s for s in range(len(slots)) if slots[s] == v) - len(slots) for v in range(3)}

        either_tail = {v: max(tail(rect_slots)[v], tail(diag_slots[True])[v]) for v in range(3)}

        FIRST_LO = {2: 5, 3: 7}
        FIRST_SPLITS = [(2.9, "w first", 2), (3.9, "hi first", 2), (4.1, "w first", 3), (5.9, "hi first", 3)]

        @block.tensor
        def _(pe):
            def turn(t):
                kind, a, half, c, j = tasks[t]
                if turn_before(t) >= 0:
                    pe.wait_ge(turn_out, turn_before(t) + 1)
                if kind == "x":
                    if j % XP == 0:
                        pe.wait_ge(x_nat_ready[c][j // XP], 16 * (x_order.index((a, half)) + 1))
                    for q in range(4):
                        mm = pe.transpose(turn_bank(t)[:, q * P:(q + 1) * P], x_nat[:, c, q, j * P:(j + 1) * P], ident[:, :])
                else:
                    o, n = out_order.index((a, half)), width(a)
                    if c == 0:
                        pe.wait_ge(pair_slot(o)[1], o_pair_loads(o))
                    for q in range(4):
                        b0 = c * BANK + q * P
                        mm = pe.transpose(turn_bank(t)[:, q * n:(q + 1) * n], pair_slot(o)[0][0:n, b0:b0 + P], ident[0:n, 0:n])
                mm.then_inc(turned, 1)

            def sum_group(units, diag, first_pos, seen, last):
                for s in (first_pos, first_pos + 1):
                    j, dm = units[s]
                    for c in range(NC):
                        side, row = sum_place(diag, dm)
                        q, r = 2 * side + c, 4 * j + row
                        mm = pe.matmul(psO[32 * q:32 * q + 32, :], pick[:, 32 - r:64 - r],
                                       prod[:, s % 4, c * BANK:(c + 1) * BANK],
                                       start=q not in seen, stop=last and s == first_pos + 1 or last and side == 0)
                        seen.add(q)
                if last:
                    mm.then_inc(sums_ready, 1)

            def one_block(units, k, u, slots, before, place, row, head):
                seen = set()
                for s, (j, dm) in enumerate(units):
                    if all(v[0] != j for v in units[:s]):
                        pe.wait_ge(w_ready, k * NJ + (j + 1))
                    if all(v[1] != dm for v in units[:s]):
                        pe.wait_ge(stack_hi_ready[dm], 16 * (row + 1))
                        pe.wait_ge(stack_lo_ready[dm], 16 * (row + 1))
                    last = max([v for v in range(s) if slots[v] == slots[s]], default=None)
                    if last is None and before is not None:
                        last = before[slots[s]]
                    if last is not None:
                        pe.wait_ge(prod_ready, u + (last + 1))
                    elif s < 3:
                        pe.wait_ge(turn_out, N_START)
                    for c in range(NC):
                        t = psT[:, slots[s], c * BANK:(c + 1) * BANK]
                        xs = stack[:, dm, c * BANK:(c + 1) * BANK]
                        pe.matmul(t, w_hi[:, j, dm * P:(dm + 1) * P], xs, start=True, stop=False)
                        mm = pe.matmul(t, w_lo[:, j, dm * P:(dm + 1) * P], xs, start=False, stop=True)
                    mm.then_inc(t_ready, 1)
                    if s % 2 == 1:
                        if s > 1:
                            pe.wait_ge(prod_ready, u + (s - 1))
                            if s == 3 and not head:
                                pe.wait_ge(sums_out, k)
                            sum_group(units, units is DIAG, s - 3, seen, False)
                        elif not head:
                            pe.wait_ge(prod_ready, u)
                            sum_group(RECT, False, UR - 2, {0, 1, 2, 3}, True)
                    for t in slot_tasks.get((place, s), []):
                        turn(t)

            pe.wait_ge(const_ready, 4)
            for t in slot_tasks["start", 0]:
                turn(t)
            for half in range(HALVES):
                for mb in range(ROWS - 1, -1, -1):
                    row = row_of(half, mb)
                    for k, u, nb, peeled in rect_blocks(pe, half, mb):
                        head = peeled and half == 0
                        before = None if head else tail(diag_slots[False]) if peeled else either_tail
                        one_block(RECT, k, u, rect_slots, before, ("first", half) if peeled else None, row, head)
                    one_block(DIAG, first_block(half, mb) + mb, first_unit(half, mb) + mb * UR, diag_slots[mb > 0],
                              tail(rect_slots if mb > 0 else diag_slots[True]), ("diag", half, mb), row, False)
            pe.wait_ge(prod_ready, first_unit(HALVES, ROWS - 1))
            sum_group(RECT, False, UR - 2, {0, 1, 2, 3}, True)
            pe.wait_ge(late_pick_ready, NC * NL)
            pe.wait_ge(sums_out, NK)
            for t in range(BANK // P):
                mm = pe.matmul(late_bank(t), o_blk[:, t * P:(t + 1) * P], late_pick[:, :, :].rearrange("p c i -> p (c i)"),
                               start=True, stop=True)
            mm.then_inc(late_ready, 1)

        @block.vector
        def _(dve):
            dve.memset(ident[:, :], 0.0).then_inc(const_zero, 1)
            dve.memset(pick[:, :], 0.0).then_inc(const_zero, 1)
            dve.memset(late_pick[:, :, :], 0.0).then_inc(const_zero, 1)
            dve.wait_ge(const_zero, 3)
            dve.memset(pick[0:64, 32:33], 1.0).then_inc(const_ready, 1)
            dve.memset(pick[64:128, 34:35], 1.0).then_inc(const_ready, 1)

            def split_x_first(p):
                dve.wait_ge(x_hi_ready, p + 1)
                wait_part_free(dve, 0, 2 * p + 1)
                dve.tensor_tensor(part(0, 2 * p + 1), x_pair(0, ROWS - 1, p), part(0, 2 * p).bitcast(F32),
                                  ALU.subtract).then_inc(x_lo_ready, 1)

            def one_block(units, slots, u, nb, half, peeled=False):
                at = [(nb * NJ + j) * HALF for j in range(NJ)]
                if not isinstance(nb, int):
                    at = [dve.snap(a) for a in at]
                for s, (j, dm) in enumerate(units):
                    if peeled and all(v[0] != j for v in units[:s]):
                        dve.wait_ge(turn_out, task_no["x", nb, half, NC - 1, j] + 1)
                    if peeled and half == 0:
                        for p in (2, 3):
                            if s == FIRST_LO[p]:
                                split_x_first(p)
                    dve.wait_ge(t_ready, u + (s + 1))
                    dve.tensor_tensor(prod[:, s % 4, :], psT[:, slots[s], :],
                                      xT[:, bass.ds(at[j], HALF)], ALU.mult).then_inc(prod_ready, 1)

            split_x_first(0)
            split_x_first(1)
            for half in range(HALVES):
                for mb in range(ROWS - 1, -1, -1):
                    for k, u, nb, peeled in rect_blocks(dve, half, mb):
                        if not peeled:
                            dve.wait_ge(turn_out, task_no["x", 0, half, NC - 1, NJ - 1] + 1)
                        one_block(RECT, rect_slots, u, nb, half, peeled)
                    one_block(DIAG, diag_slots[mb > 0], first_unit(half, mb) + mb * UR, mb, half)
            dve.wait_ge(late_ready, 1)
            dve.wait_ge(turn_out, len(tasks))
            put_late(range(BANK // P // 2), dve.tensor_copy, late_dve)


        HI_POS = [[-0.5, -0.4, 8.0, 12.9], [-0.5, -0.4, 9.4, 12.7]]
        LO_POS = [[-0.5, 3.5, 12.0, 16.0], [0.0, 4.0, 7.5, 13.9]]
        HI_COPY = [0.1, 0.0, 3.0, 7.6, 8.9, 12.6, 14.1, 15.7]
        LO_COPY = [[5.3, 6.3, 7.1, 8.8, 15.1, 15.1, 20.4, 20.4], [5.3, 5.3, 7.1, 8.8, 13.0, 13.3, 19.0, 16.0]]

        def follow(units, place, diag, more):
            work = []
            if more:
                work += [(last_use(units, 0, j) + 0.6, "w", j) for j in range(NJ)]
                if diag:
                    table = diag[1] == 1
                    work += [(HI_POS[table][p], "hi", p) for p in range(BLK // 2)]
                    work += [(LO_POS[table][p], "lo", p) for p in range(BLK // 2)]
            work += [(i + 0.8, "turn", t) for (p, i), ts in slot_tasks.items() if p == place and p for t in ts]
            work.append((1.7, "sums", 0))
            if place == ("first", 0):
                work += FIRST_SPLITS
            if diag and diag[1] == 0:
                work.append((1.8, "w of this", NJ - 1))
            return sorted(work)

        def next_row(half, mb):
            return (half, mb - 1) if mb else (half + 1, ROWS - 1)

        @block.scalar
        def _(act):
            def split_w(k, u_free, j):
                act.wait_ge(w_raw_ready[j % 2], (k * 2 + (j // 2 + 1)) * 32)
                if u_free is not None:
                    act.wait_ge(t_ready, u_free)
                act.activation(w_hi[:, j, :].rearrange("p (m a e) -> p m a e", a=2, e=E),
                               w_raw[:, j % 2, :].rearrange("p (a m e) -> p m a e", a=2, e=E),
                               ACT.Copy).then_inc(w_hi_ready, 1)

            def split_x(half, mb, p):
                act.wait_ge(turn_out, task_no["x", mb, half, NC - 1, p] + 1)
                wait_part_free(act, row_of(half, mb), 2 * p)
                act.activation(part(row_of(half, mb), 2 * p), x_pair(half, mb, p), ACT.Copy).then_inc(x_hi_ready, 1)

            def take_turned(t):
                kind, a, half, c, j = tasks[t]
                if kind == "x":
                    if half > 0:
                        act.wait_ge(prod_ready, first_unit(half - 1, a) + first_unit_rows(a))
                    dst = xT[:, (a * NJ + j) * HALF + c * BANK:(a * NJ + j) * HALF + (c + 1) * BANK]
                    src = turn_bank(t)
                else:
                    o, n = out_order.index((a, half)), width(a)
                    if 0 < o < len(out_order) - N_XT:
                        act.wait_ge(stored, 16 * o)
                    dst = nat_slot(o)[:, 4 * c:4 * c + 4, 0:n]
                    src = turn_bank(t)[:, 0:4 * n].rearrange("p (q n) -> p q n", n=n)
                act.wait_ge(turned, t + 1)
                act.activation(dst, src, ACT.Copy).then_inc(turn_out, 1)

            def take_sums(k):
                act.wait_ge(sums_ready, k + 1)
                act.wait_ge(scratch_ready, k * 128)
                act.activation(o_blk[:, :], psO[:, :], ACT.Copy).then_inc(sums_out, 1)

            def one_block(units, k, u, place, diag=None, head=False, more=True):
                for pos, what, i in follow(units, place, diag, more):
                    if what == "w":
                        if not (diag and diag[1] == 1 and i == NJ - 1):
                            split_w(k + 1, u + (last_use(units, 0, i) + 1), i)
                    elif what == "w of this":
                        split_w(k, u, i)
                    elif what == "hi":
                        split_x(*next_row(*diag), i)
                    elif what == "turn":
                        take_turned(i)
                    elif what == "w first":
                        split_w(0, None, i)
                    elif what == "hi first":
                        split_x(0, ROWS - 1, i)
                    elif what == "sums" and not head:
                        take_sums(k - 1)

            turns = slot_tasks["start", 0]
            for t in turns[:NJ + 1]:
                take_turned(t)
            split_x(0, ROWS - 1, 0)
            split_w(0, None, 0)
            take_turned(turns[NJ + 1])
            split_x(0, ROWS - 1, 1)
            for t in turns[NJ + 2:]:
                take_turned(t)
            split_w(0, None, 1)
            for half in range(HALVES):
                for mb in range(ROWS - 1, -1, -1):
                    for k, u, nb, peeled in rect_blocks(act, half, mb):
                        one_block(RECT, k, u, ("first", half) if peeled else None, head=peeled and half == 0)
                    k = first_block(half, mb) + mb
                    one_block(DIAG, k, first_unit(half, mb) + mb * UR, ("diag", half, mb), (half, mb), more=k + 1 < NK)
            take_sums(NK - 1)
            act.wait_ge(late_ready, 1)
            act.wait_ge(turn_out, len(tasks))
            put_late(range(BANK // P // 2, BANK // P), lambda dst, src: act.activation(dst, src, ACT.Copy), late_act)

        @block.gpsimd
        def _(pool):
            pool.wait_ge(const_zero, 3)
            pool.affine_select(out=ident[:, :], in_=ident[:, :], compare_op=ALU.not_equal, fill=1.0, base=0,
                               pattern=[[-1, P]], channel_multiplier=1).then_inc(const_ready, 2)

            def split_w(k, j):
                pool.wait_ge(w_hi_ready, k * NJ + (j + 1))
                pool.tensor_tensor(w_lo[:, j, :].rearrange("p (m a e) -> p m a e", a=2, e=E),
                                   w_raw[:, j % 2, :].rearrange("p (a m e) -> p m a e", a=2, e=E),
                                   w_hi[:, j, :].bitcast(F32).rearrange("p (m a e) -> p m a e", a=2, e=E),
                                   ALU.subtract).then_inc(w_ready, 1)

            def split_x(half, mb, p):
                row = row_of(half, mb)
                pool.wait_ge(x_hi_ready, BLK // 2 * row + p + 1)
                wait_part_free(pool, row, 2 * p + 1)
                pool.tensor_tensor(part(row, 2 * p + 1), x_pair(half, mb, p), part(row, 2 * p).bitcast(F32),
                                   ALU.subtract).then_inc(x_lo_ready, 1)

            for j in range(NJ):
                split_w(0, j)
            for half in range(HALVES):
                for mb in range(ROWS - 1, -1, -1):
                    for k, u, nb, peeled in rect_blocks(pool, half, mb):
                        for j in range(NJ):
                            split_w(k + 1, j)
                    k = first_block(half, mb) + mb
                    for pos, what, i in follow(DIAG, None, (half, mb), k + 1 < NK):
                        if what == "w":
                            split_w(k + 1, i)
                        elif what == "lo":
                            split_x(*next_row(half, mb), i)

            for c in range(NC):
                for i, (n, m) in enumerate(late_pairs):
                    side, row = sum_place(True, m)
                    col = late_pick[:, c, i:i + 1]
                    pool.affine_select(out=col, in_=col, compare_op=ALU.not_equal, fill=1.0,
                                       base=-(32 * (2 * side + c) + 2 * n + row), pattern=[[0, 1]],
                                       channel_multiplier=1).then_inc(late_pick_ready, 1)

        @block.sync
        def _(sp):
            blocks = [(half, mb, nb) for half in range(HALVES) for mb in range(ROWS - 1, -1, -1)
                      for nb in list(range(mb - 1, -1, -1)) + [mb]]

            def load_w(k, j):
                half, mb, nb = blocks[k]
                if 4 * k + j >= 2:
                    sp.wait_ge(w_ready, 4 * k + j - 1)
                d0 = 2 * j + 1 if nb == mb else 0
                for a in range(2):
                    i = pair(BLK * nb + 2 * j + a, BLK * mb + d0)
                    sp.dma_start(w_raw[:, j % 2, (a * BLK + d0) * E:(a + 1) * BLK * E],
                                 w[:, i:i + BLK - d0, :].rearrange("f i e -> f (i e)").partition_broadcast(2)
                                 ).then_inc(w_raw_ready[j % 2], 16)

            def load_x(xb, half, c, part):
                o = x_order.index((xb, half))
                if o > 0:
                    pxb, ph = x_order[o - 1]
                    sp.wait_ge(turned, task_no["x", pxb, ph, c, XP * part + XP - 1] + 1)
                b0, n0 = half * HALF + c * BANK, BLK * xb + 2 * XP * part
                sp.dma_start(x_nat[:, c, :, 2 * XP * E * part:2 * XP * E * (part + 1)],
                             x[b0:b0 + BANK, n0:n0 + 2 * XP, :].rearrange("(t p) n e -> p t (n e)", p=P)
                             ).then_inc(x_nat_ready[c][part], 16)

            def copy_part(row, u_free, dm, lo):
                item = dm // 2 * 2 + lo
                sp.wait_ge(x_lo_ready if lo else x_hi_ready, BLK // 2 * row + dm // 2 + 1)
                if u_free is not None:
                    sp.wait_ge(t_ready, u_free)
                here = 64 * (dm % 2)
                to = 64 - here if lo else here
                sp.dma_start(stack[to:to + 64, dm, :].bitcast(F32), part(row, item)[here:here + 64, :].bitcast(F32)
                             ).then_inc((stack_lo_ready if lo else stack_hi_ready)[dm], 16)

            def write_sums(k):
                half, mb, nb = blocks[k]
                sp.wait_ge(sums_out, k + 1)
                for q in range(4):
                    side, c = q // 2, q % 2
                    b0 = half * HALF + c * BANK
                    dst = scratch[BLK * nb:BLK * nb + BLK, BLK * mb:BLK * mb + BLK, b0:b0 + BANK]
                    for h in range(2):
                        p0 = 32 * q + 16 * h
                        sp.dma_start(dst[:, members(nb == mb, side, h), :], o_blk[p0:p0 + 16, :]).then_inc(scratch_ready, 16)

            def load_pairs(o, k_last):
                g, half = out_order[o]
                sp.wait_ge(scratch_ready, 128 * (k_last + 1))
                if 1 <= o < len(out_order) - N_XT:
                    pg, ph = out_order[o - 1]
                    sp.wait_ge(turned, task_no["out", pg, ph, NC - 1, 0] + 1)
                elif o > 0:
                    sp.wait_ge(prod_ready, first_unit(HALVES, ROWS - 1) - UD)
                for p0, n, m, cnt in parts_of(o):
                    sp.dma_start(pair_slot(o)[0][p0:p0 + cnt, :],
                                 scratch[n, m:m + cnt, half * HALF:(half + 1) * HALF]).then_inc(pair_slot(o)[1], 16)

            def store(o, c=None):
                g, half = out_order[o]
                lo, hi = (0, NC) if c is None else (c, c + 1)
                sp.wait_ge(turn_out, task_no["out", g, half, hi - 1, 0] + 1)
                if (g, half) in end_groups:
                    n_late = sum(len(late_runs(v)) for v, _ in end_groups[:end_groups.index((g, half)) + 1])
                    sp.wait_ge(late_dve, n_late * (BANK // P // 2))
                    sp.wait_ge(late_act, n_late * (BANK // P // 2))
                rows = out[half * HALF + lo * BANK:half * HALF + hi * BANK, 0, P * g:P * g + width(g)]
                sp.dma_start(rows.rearrange("(t p) i -> p t i", p=P),
                             nat_slot(o)[:, 4 * lo:4 * hi, 0:width(g)]).then_inc(stored, 16)

            def copy_parts(pairs):
                for p in pairs:
                    for dm, lo in ((2 * p, 0), (2 * p + 1, 0), (2 * p, 1), (2 * p + 1, 1)):
                        copy_part(0, None, dm, lo)

            for c in range(NC):
                for part_no in range(NJ // XP):
                    load_x(ROWS - 1, 0, c, part_no)
            load_w(0, 0)
            for c in range(NC):
                load_x(ROWS - 2, 0, c, 0)
            load_w(0, 1)
            copy_parts([0])
            for c in range(NC):
                load_x(ROWS - 2, 0, c, 1)
            load_w(0, 2)
            copy_parts([1])

            spare = {k: [] for k in range(NK + 1)}
            for o, (g, h) in enumerate(out_order):
                place, i = next(at for at, ts in slot_tasks.items() if task_no["out", g, h, NC - 1, 0] in ts)
                k = first_block(place[1], place[2]) + place[2] if place[0] == "diag" else first_block(place[1], ROWS - 1)
                if (g, h) in end_groups:
                    spare[k].append((1.76, "pairs", o))
                    continue
                elif place[0] == "diag" and place[2] > 0 and (place[2] < ROWS - 1 or i < UD // 2):
                    spare[k - 1].append((10.0, "pairs", o))
                else:
                    spare[k].append((1.8 if k == NK - 1 else max(5.0, i - 11.1), "pairs", o))
                if k + 1 < NK and (i > UR // 2 or place[0] == "diag" and i > UD // 2):
                    spare[k + 1].append((7.0 if k + 2 < NK else 1.7, "store", o))
                else:
                    spare[k].append((i + 0.9, "store", o))
            PARTS = [(c, part_no) for c in range(NC) for part_no in range(NJ // XP)]
            for half in range(1, HALVES):
                for c, q in PARTS:
                    spare[first_block(half - 1, ROWS - 1) + 1].append((-1 + c, "x", (ROWS - 1, half, c, q)))
                    for mb in range(ROWS - 2, 1, -1):
                        spare[first_block(half - 1, mb - 1)].append((10 + 4 * c, "x", (mb, half, c, q)))
                    for mb in (1, 0):
                        spare[first_block(half - 1, mb) + mb].append((19.0 + 0.4 * c if mb else 14.0 + 2.9 * c, "x", (mb, half, c, q)))
            spare[0] += [(2.0, "w first", 3), (5.5, "copy first", 2), (7.5, "copy first", 3)]
            for xb in range(ROWS - 3, -1, -1):
                for c, q in PARTS:
                    before = task_no["x", xb + 1, 0, c, XP * q + XP - 1]
                    at = next((i for (p, i), ts in slot_tasks.items() if p == ("first", 0) and before in ts), 3.0)
                    spare[0].append((at + 0.9, "x", (xb, 0, c, q)))
            for k, (half, mb, nb) in enumerate(blocks):
                diag, peeled = nb == mb, k == first_block(half, ROWS - 1)
                units = DIAG if diag else RECT
                place = ("diag", half, mb) if diag else ("first", half) if peeled else None
                row = row_of(half, mb)
                work = []
                if k + 1 < NK:
                    work += [(3.0, "w", 0), (3.2, "w", 1)] if k else [(10.0, "w", 0), (11.5, "w", 1)]
                    work += [(last_use(units, 0, j) + 3.0, "w", j + 2) for j in range(2)]
                    if diag:
                        work += [(HI_COPY[dm], "copy", (row, dm, 0)) for dm in range(BLK)]
                        work += [(LO_COPY[mb == 1][dm], "copy", (row, dm, 1)) for dm in range(BLK)]
                if k == NK - 1:
                    sums_pos = 1.75
                elif diag:
                    sums_pos = 5.7 if mb == 1 else 9.8
                else:
                    sums_pos = 0.9
                if k > 0:
                    work.append((sums_pos, "sums", k - 1))
                work += spare[k]
                late = [(pos - len(units), what, i) for pos, what, i in work if pos >= len(units) + 1]
                if k + 1 < NK and not (diag and mb == 1):
                    spare[k + 1] += late
                    work = [v for v in work if v[0] < len(units) + 1]
                for pos, what, i in sorted(work, key=lambda v: v[0]):
                    if what == "w":
                        load_w(k + 1, i)
                    elif what == "copy":
                        done_row, dm, lo = i
                        h, b = divmod(done_row, ROWS)
                        u = first_unit(h, ROWS - 1 - b) + (ROWS - 1 - b) * UR
                        copy_part(done_row + 1, u + (last_use(DIAG, 1, dm) + 1), dm, lo)
                    elif what == "sums":
                        write_sums(i)
                    elif what == "pairs":
                        load_pairs(i, k - 2 if pos < sums_pos or out_order[i] in end_groups else k - 1)
                    elif what == "store":
                        store(i)
                    elif what == "w first":
                        load_w(0, i)
                    elif what == "copy first":
                        copy_parts([i])
                    else:
                        load_x(*i)
            for g, h in end_groups:
                for c in range(NC):
                    store(out_order.index((g, h)), c)
            sp.wait_ge(stored, 16 * (len(out_order) + (NC - 1) * len(end_groups)))


def kernel(r_inputs, L0_rec_param):
    import numpy as np
    import concourse.bacc as bacc
    from concourse.bass_utils import run_bass_kernel_spmd

    nc = bacc.Bacc("TRN2", target_bir_lowering=False, num_devices=1)
    x = np.ascontiguousarray(r_inputs)
    w = np.ascontiguousarray(L0_rec_param)
    x_ap = nc.dram_tensor("x", x.shape, F32, kind="ExternalInput").ap()
    w_ap = nc.dram_tensor("w", w.shape, F32, kind="ExternalInput").ap()
    out_ap = nc.dram_tensor("out", (x.shape[0], 1, w.shape[1]), F32, kind="ExternalOutput").ap()
    build(nc, x_ap, w_ap, out_ap)
    r = run_bass_kernel_spmd(nc, [{"x": x, "w": w}], core_ids=[0])
    return r.results[0]["out"]
```
